# Optimizing a Trainium2 kernel written in Bass

```python
import numpy as np
import jax
import jax.numpy as jnp

def _softmax(x, axis=-1):
    return jax.nn.softmax(x, axis=axis)
def _gelu(x):
    return jax.nn.gelu(x, approximate=True)
def _silu(x):
    return jax.nn.silu(x)
def _sigmoid(x):
    return jax.nn.sigmoid(x)
def _layernorm(x, axis=-1, eps=1e-5):
    m = jnp.mean(x, axis=axis, keepdims=True)
    v = jnp.var(x, axis=axis, keepdims=True)
    return (x - m) / jnp.sqrt(v + eps)
def _scatter_add(tgt, idx, src, axis=0):
    return tgt.at[idx].add(src)
def _segment_sum(src, seg, n):
    return jax.ops.segment_sum(src, seg, n)

kernel_name = 'mk_conv_preact_d1_conv_nhwc256_5f45c2'

def setup_inputs(seed: int = 0):
    np.random.seed(seed)
    _w = jnp.asarray
    def _rec_inputs():
        import jax
        import jax.numpy as jnp
        _gk = jax.random.key(seed)
        x = -8.268e-05 + 0.9999 * jax.random.normal(jax.random.fold_in(_gk, 1), (16, 112, 112, 256), jnp.float32)
        return x
    x = _rec_inputs()
    def _L0_conv_setup():
        import jax, jax.numpy as jnp
        import numpy as np

        @jax.custom_vjp
        def ste_sign(x):
            return jnp.where(x >= 0, jnp.ones((), x.dtype), -jnp.ones((), x.dtype))

        def _ste_fwd(x):
            return (ste_sign(x), x)

        def _ste_bwd(x, g):
            return (g * (jnp.abs(x) <= 1).astype(g.dtype),)
        ste_sign.defvjp(_ste_fwd, _ste_bwd)
        key = jax.random.key(seed)
        k1, k2 = jax.random.split(key)
        x = jax.random.normal(k1, (16, 112, 112, 256), dtype=jnp.float32)
        kernel = jax.random.normal(k2, (3, 3, 256, 1), dtype=jnp.float32) * 0.1
        return {'x': x, 'kernel': kernel}
    _L0_conv_all = _L0_conv_setup()
    _L0_conv_in = {k: v for k, v in _L0_conv_all.items() if k in ('kernel', )}
    del _L0_conv_all

    return {
        "x": x,
        "L0_conv_kernel": _L0_conv_in["kernel"],
    }

def reference(x, L0_conv_kernel):
    import jax
    import jax.numpy as jnp
    def _L0_conv_ref(x, kernel):
        import jax, jax.numpy as jnp
        import numpy as np

        @jax.custom_vjp
        def ste_sign(x):
            return jnp.where(x >= 0, jnp.ones((), x.dtype), -jnp.ones((), x.dtype))

        def _ste_fwd(x):
            return (ste_sign(x), x)

        def _ste_bwd(x, g):
            return (g * (jnp.abs(x) <= 1).astype(g.dtype),)
        ste_sign.defvjp(_ste_fwd, _ste_bwd)
        xq = ste_sign(x)
        kq = ste_sign(kernel)
        kh, kw, C, mult = kernel.shape
        rhs = kq.reshape(kh, kw, 1, C * mult)
        out = jax.lax.conv_general_dilated(xq, rhs, window_strides=(1, 1), padding='SAME', feature_group_count=C, dimension_numbers=('NHWC', 'HWIO', 'NHWC'))
        return out

    def _gn(v, G=32, eps=1e-5):
        B_, H_, W_, C_ = v.shape
        g = v.reshape(B_, H_, W_, G, C_ // G)
        m = jnp.mean(g, axis=(1, 2, 4), keepdims=True)
        s = jnp.var(g, axis=(1, 2, 4), keepdims=True)
        return ((g - m) / jnp.sqrt(s + eps)).reshape(v.shape)

    def _ln_c(v, eps=1e-6):
        m = jnp.mean(v, axis=-1, keepdims=True)
        s = jnp.var(v, axis=-1, keepdims=True)
        return (v - m) / jnp.sqrt(s + eps)

    def _ln_t(v, eps=1e-5):
        m = jnp.mean(v, axis=-1, keepdims=True)
        s = jnp.var(v, axis=-1, keepdims=True)
        return (v - m) / jnp.sqrt(s + eps)

    def _to_tokens(v):
        B_, H_, W_, C_ = v.shape
        return v.reshape(B_, H_ * W_, C_)
    def _from_tokens(t, like):
        return t.reshape(like.shape)

    x = x + _L0_conv_ref(_gn(x), L0_conv_kernel)
    return x


_drawn_inputs = setup_inputs


def setup_inputs(seed=0):
    import zlib

    import numpy as np

    out = dict(_drawn_inputs(seed))
    spreads = {}
    factors = {}
    for name, (base, spread) in spreads.items():
        noise = np.random.default_rng([zlib.crc32(name.encode()), seed]).standard_normal(out[name].shape)
        drawn = base * np.exp(spread * noise) if base else spread * noise
        out[name] = jnp.asarray(drawn.astype(out[name].dtype))
    for name, factor in factors.items():
        out[name] = (out[name] * factor).astype(out[name].dtype)
    return out
```

```python
from contextlib import ExitStack

import concourse.bass as bass
from concourse import mybir

F32 = mybir.dt.float32
BF16 = mybir.dt.bfloat16
FP8 = mybir.dt.float8e4
U8 = mybir.dt.uint8
U32 = mybir.dt.uint32
ALU = mybir.AluOpType
ACT = mybir.ActivationFunctionType

IMAGES, H, W, C = 16, 112, 112, 256
TAPS = 3
GC = 8
HALVES = 2
HC = C // HALVES
GROUPS = HC // GC
UNITS = HALVES * IMAGES
SLOTS = 3
CHUNKS = 8
CW = W // CHUNKS
QUAD = 4
QUADS = GROUPS // QUAD
MEAN_LEAD = 3
LEAD = 2
SIGN_BUFS = 4
CONV_BUFS = 2
MATS = TAPS * GC
FULL = 128
GROUP_BYTES = MATS * H + FULL - H
PERIOD = 8


def conv_preact(nc: bass.Bass, x: bass.AP, kern: bass.AP, out: bass.AP):
    kern_rows = kern.rearrange("a b c m -> a (b c m)")
    TC = TAPS * C

    with ExitStack() as ctx:
        def sb(name, shape, dt):
            return ctx.enter_context(nc.sbuf_tensor(name, shape, dt))

        def sem(name):
            return ctx.enter_context(nc.semaphore(name))

        slots = sb("slots", [H, SLOTS, W, HC], F32)
        bands = sb("bands", [H, GROUPS * GROUP_BYTES], FP8)
        pattern = sb("pattern", [H, C // GC, MATS, PERIOD], FP8)
        signs = sb("signs", [H, SIGN_BUFS, W + 2, GC], FP8)
        sums = sb("sums", [H, SLOTS, GROUPS], F32)
        averager = sb("averager", [H, H], F32)
        in_band = sb("in_band", [H, H], F32)
        mask = sb("mask", [H, H], U8)

        conv = [ctx.enter_context(nc.psum_tensor(f"conv{i}", [FULL, GC, FULL], F32))
                for i in range(CONV_BUFS)]
        means = [ctx.enter_context(nc.psum_tensor(f"means{q}", [H, 512], F32))
                 for q in range(2)]
        unread = sb("unread", [H, 2, W, GC], U8)

        loaded = [sem(f"loaded{s}") for s in range(SLOTS)]
        stored = [[sem(f"stored{s}_{j}") for j in range(CHUNKS)] for s in range(SLOTS)]
        taps_cleared = sem("taps_cleared")
        taps_loaded = sem("taps_loaded")
        averager_ready = sem("averager_ready")
        borders_ready = sem("borders_ready")
        mask_step = sem("mask_step")
        pads_ready = sem("pads_ready")
        pattern_step = sem("pattern_step")
        bands_ready = sem("bands_ready")
        sums_ready = sem("sums_ready")
        means_ready = sem("means_ready")
        signs_ready = sem("signs_ready")
        conv_ready = sem("conv_ready")
        added = sem("added")

        taps = bands[:, 0:PERIOD * TC * 4].bitcast(F32).rearrange("p (x j) -> p x j", x=PERIOD)
        band_words = bands[:, :].bitcast(U32).rearrange("p (g n) -> p g n", g=GROUPS)
        pattern_words = pattern[:, :, :, :].rearrange("p g m b -> p g (m b)").bitcast(U32)
        mask_words = mask[:, :].bitcast(U32)
        PW = PERIOD // 4

        block = ctx.enter_context(nc.Block())

        def dram_chunk(t, u, j):
            half, image = u // IMAGES, u % IMAGES
            if isinstance(u, int):
                return t[image, :, j * CW:(j + 1) * CW, half * HC:(half + 1) * HC]
            return t[bass.ds(image, 1), :, j * CW:(j + 1) * CW,
                     bass.ds(half * HC, HC)].rearrange("a h w c -> (a h) w c")

        @block.sync
        def _(sp):
            def load(u, slot, j):
                sp.dma_start(slots[:, slot, j * CW:(j + 1) * CW, :],
                             dram_chunk(x, u, j)).then_inc(loaded[slot], 16)

            def store(u, slot, j):
                sp.dma_start(dram_chunk(out, u, j),
                             slots[:, slot, j * CW:(j + 1) * CW, :]).then_inc(stored[slot][j], 16)

            def turn(u, slot, round_, refill):
                sp.wait_ge(added, GROUPS * (u + 1))
                for j in range(CHUNKS + 2):
                    if j < CHUNKS:
                        store(u, slot, j)
                    if refill and j >= 2:
                        sp.wait_ge(stored[slot][j - 2], 16 * (round_ + 1))
                        load(u + SLOTS, slot, j - 2)

            for u in range(SLOTS):
                for j in range(CHUNKS):
                    load(u, u, j)
            refills = UNITS - SLOTS
            rounds = refills // SLOTS
            with sp.Fori(0, rounds) as r:
                for s in range(SLOTS):
                    turn(r * SLOTS + s, s, r, True)
            for u in range(rounds * SLOTS, UNITS):
                turn(u, u % SLOTS, u // SLOTS, u < refills)
            for s in range(SLOTS):
                for j in range(CHUNKS):
                    sp.wait_ge(stored[s][j], 16 * len(range(s, UNITS, SLOTS)))

        @block.gpsimd
        def _(pool):
            nc.gpsimd.memset(averager[:, :], 1.0 / (H * W * GC)).then_inc(averager_ready, 1)
            nc.gpsimd.memset(in_band[:, :], 255.0).then_inc(mask_step, 1)
            pool.wait_ge(mask_step, 1)
            nc.gpsimd.affine_select(out=in_band[:, :], in_=in_band[:, :], compare_op=ALU.is_ge,
                                    fill=0.0, base=1, pattern=[[1, H]],
                                    channel_multiplier=-1).then_inc(mask_step, 1)
            pool.wait_ge(mask_step, 2)
            nc.gpsimd.affine_select(out=in_band[:, :], in_=in_band[:, :], compare_op=ALU.is_ge,
                                    fill=0.0, base=1, pattern=[[-1, H]],
                                    channel_multiplier=1).then_inc(mask_step, 1)
            pool.wait_ge(mask_step, 3)
            nc.gpsimd.tensor_copy(mask[:, :], in_band[:, :]).then_inc(mask_step, 1)
            for b in range(SIGN_BUFS):
                nc.gpsimd.memset(signs[:, b, 0, :], 0.0)
                nc.gpsimd.memset(signs[:, b, W + 1, :], 0.0).then_inc(borders_ready, 1)

        @block.scalar
        def _(act):
            act.wait_ge(taps_cleared, 1)
            for r in range(PERIOD):
                for dh in range(TAPS):
                    place = (r + 1 - dh) % PERIOD
                    act.dma_start(taps[r:H:PERIOD, place, :],
                                  kern_rows[dh:dh + 1, :].to_broadcast([H // PERIOD, TC])
                                  ).then_inc(taps_loaded, 16)

            def unit_sums(u, slot, round_, after_first=True):
                act.wait_ge(loaded[slot], 16 * CHUNKS * (round_ + 1))
                for g in range(GROUPS):
                    if after_first or g >= 2:
                        act.wait_ge(sums_ready, u * GROUPS + g - 1)
                    nc.scalar.activation(unread[:, g % 2, :, :],
                                         slots[:, slot, :, g * GC:(g + 1) * GC], ACT.Copy,
                                         accum_out=sums[:, slot, g:g + 1]).then_inc(sums_ready, 1)

            for u in range(SLOTS):
                unit_sums(u, u, 0, after_first=u > 0)
            with act.Fori(1, UNITS // SLOTS) as r:
                for s in range(SLOTS):
                    unit_sums(r * SLOTS + s, s, r)
            for u in range(UNITS // SLOTS * SLOTS, UNITS):
                unit_sums(u, u % SLOTS, u // SLOTS)


        @block.tensor
        def _(pe):
            pe.wait_ge(averager_ready, 1)
            pe.wait_ge(borders_ready, SIGN_BUFS)
            pe.wait_ge(pads_ready, 1)

            def unit_means(u, slot, q):
                pe.wait_ge(sums_ready, u * GROUPS + QUAD * (q + 1))
                nc.tensor.matmul(means[q % 2][:, 0:QUAD], averager[:, :],
                                 sums[:, slot, q * QUAD:(q + 1) * QUAD],
                                 start=True, stop=True).then_inc(means_ready, 1)

            def unit(u, slot, after_first=True, last=False):
                half = u // IMAGES
                for g in range(GROUPS):
                    n = u * GROUPS + g
                    if g % QUAD == QUAD - MEAN_LEAD:
                        if g < GROUPS - MEAN_LEAD:
                            unit_means(u, slot, g // QUAD + 1)
                        elif not last:
                            unit_means(u + 1, (slot + 1) % SLOTS, 0)
                    pe.wait_ge(bands_ready, half * GROUPS + g + 1)
                    pe.wait_ge(signs_ready, n + 1)
                    if after_first or g >= CONV_BUFS:
                        pe.wait_ge(added, n + 1 - CONV_BUFS)
                    pe.nop(nofuse=True)
                    for c in range(GC):
                        for dw in range(TAPS):
                            at = g * GROUP_BYTES + (dw * GC + c) * H
                            product = nc.tensor.matmul(conv[g % CONV_BUFS][:, c, 0:W],
                                                       bands[:, at:at + FULL],
                                                       signs[:, g % SIGN_BUFS, dw:dw + W, c],
                                                       start=dw == 0, stop=dw == TAPS - 1)
                    product.then_inc(conv_ready, 1)

            unit_means(0, 0, 0)
            unit(0, 0, after_first=False)
            lead = (UNITS - 2) // SLOTS * SLOTS
            with pe.Fori(0, lead // SLOTS) as r:
                for s in range(SLOTS):
                    unit(r * SLOTS + s + 1, (s + 1) % SLOTS)
            for u in range(lead + 1, UNITS):
                unit(u, u % SLOTS, last=u == UNITS - 1)

        @block.vector
        def _(dve):
            nc.vector.memset(taps[:, :, :], 0.0).then_inc(taps_cleared, 1)
            dve.wait_ge(taps_loaded, 16 * PERIOD * TAPS)
            nc.vector.tensor_scalar(taps[:, :, :], taps[:, :, :], 0.0, 4.0,
                                    ALU.is_ge, ALU.mult).then_inc(pattern_step, 1)
            dve.wait_ge(pattern_step, 1)
            for dw in range(TAPS):
                nc.vector.tensor_scalar(
                    pattern[:, :, dw * GC:(dw + 1) * GC, :],
                    taps[:, :, dw * C:(dw + 1) * C].rearrange("p x (g c) -> p g c x", c=GC),
                    2.0, None, ALU.subtract, saturate=False).then_inc(pattern_step, 1)
            dve.wait_ge(pattern_step, 1 + TAPS)
            pads = band_words[:, :, MATS * H // 4:]
            nc.vector.memset(pads, 0).then_inc(pads_ready, 1)
            dve.wait_ge(mask_step, 4)

            def build(half, g):
                dst = band_words[:, g, 0:MATS * H // 4].rearrange("p (m a b) -> p m a b",
                                                                  m=MATS, b=PW)
                src = pattern_words[:, half * GROUPS + g, :].rearrange("p (m b) -> p m b", b=PW)
                src = src.unsqueeze(2).to_broadcast([H, MATS, H // PERIOD, PW])
                msk = mask_words.rearrange("p (a b) -> p a b", b=PW)
                msk = msk.unsqueeze(1).to_broadcast([H, MATS, H // PERIOD, PW])
                nc.vector.tensor_tensor(dst, msk, src, ALU.bitwise_and).then_inc(bands_ready, 1)

            def sign(u, slot, g):
                if g % QUAD == 0:
                    dve.wait_ge(means_ready, u * QUADS + g // QUAD + 1)
                    dve.nop(nofuse=True)
                nc.vector.tensor_scalar(signs[:, g % SIGN_BUFS, 1:W + 1, :],
                                        slots[:, slot, :, g * GC:(g + 1) * GC],
                                        means[g // QUAD % 2][:, g % QUAD:g % QUAD + 1], 0.5,
                                        ALU.is_ge, ALU.subtract,
                                        saturate=False).then_inc(signs_ready, 1)

            def add(u, slot, g):
                dve.wait_ge(conv_ready, u * GROUPS + g + 1)
                here = slots[:, slot, :, g * GC:(g + 1) * GC]
                nc.vector.tensor_tensor(here, here,
                                        conv[g % CONV_BUFS][0:H, :, 0:W].rearrange("p c w -> p w c"),
                                        ALU.add).then_inc(added, 1)

            def unit(u, slot, build_now=False, build_next=False, last=False):
                for g in range(GROUPS):
                    ahead = g + LEAD
                    if ahead < GROUPS:
                        if build_now:
                            build(0, ahead)
                        sign(u, slot, ahead)
                    elif not last:
                        sign(u + 1, (slot + 1) % SLOTS, ahead - GROUPS)
                    add(u, slot, g)
                    if build_next:
                        build(1, g)

            for g in range(LEAD):
                build(0, g)
                sign(0, 0, g)
            unit(0, 0, build_now=True)
            first = IMAGES - 1
            loops = (first - 1) // SLOTS
            with dve.Fori(0, loops) as r:
                for s in range(SLOTS):
                    unit(r * SLOTS + (s + 1), (s + 1) % SLOTS)
            for u in range(loops * SLOTS + 1, first + 1):
                unit(u, u % SLOTS, build_next=u == first)
            loops = (UNITS - 1 - IMAGES) // SLOTS
            with dve.Fori(0, loops) as r:
                for s in range(SLOTS):
                    unit(r * SLOTS + (IMAGES + s), (IMAGES + s) % SLOTS)
            for u in range(IMAGES + loops * SLOTS, UNITS):
                unit(u, u % SLOTS, last=u == UNITS - 1)


def kernel(x, L0_conv_kernel):
    import numpy as np
    import concourse.bacc as bacc
    from concourse.bass_utils import run_bass_kernel_spmd

    nc = bacc.Bacc("TRN2", target_bir_lowering=False, num_devices=1, dynamic_dma_scratch_size=1024)
    arrays = {"x_dram": np.ascontiguousarray(x), "kern_dram": np.ascontiguousarray(L0_conv_kernel)}
    ins = [nc.dram_tensor(n, a.shape, mybir.dt.from_np(a.dtype), kind="ExternalInput").ap()
           for n, a in arrays.items()]
    out = nc.dram_tensor("out_dram", x.shape, F32, kind="ExternalOutput").ap()
    conv_preact(nc, *ins, out)
    r = run_bass_kernel_spmd(nc, [arrays], core_ids=[0])
    return r.results[0]["out_dram"]
```

```python
from contextlib import ExitStack

import concourse.bass as bass
from concourse import mybir

F32 = mybir.dt.float32
FP8 = mybir.dt.float8e4
U8 = mybir.dt.uint8
U32 = mybir.dt.uint32
ALU = mybir.AluOpType
ACT = mybir.ActivationFunctionType

IMAGES, H, W, C = 16, 112, 112, 256
TAPS = 3
GC = 8
HALVES = 2
HC = C // HALVES
GROUPS = HC // GC
UNITS = HALVES * IMAGES
SLOTS = 3
CHUNKS = 4
CW = W // CHUNKS
FIRST_CHUNKS = 1
STORE_LEAD = 1
PAIR = 2
PAIRS = GROUPS // PAIR
MEAN_LEAD = 2
LEAD = 2
SIGN_BUFS = 4
CONV_BUFS = 3
MATS = TAPS * GC
FULL = 128
GROUP_BYTES = MATS * H + FULL - H
PERIOD = 8


def conv_preact(nc: bass.Bass, x: bass.AP, kern: bass.AP, out: bass.AP):
    kern_rows = kern.rearrange("a b c m -> a (b c m)")
    TC = TAPS * C

    with ExitStack() as ctx:
        def sb(name, shape, dt):
            return ctx.enter_context(nc.sbuf_tensor(name, shape, dt))

        def sem(name):
            return ctx.enter_context(nc.semaphore(name))

        slots = sb("slots", [H, SLOTS, W, HC], F32)
        bands = sb("bands", [H, GROUPS * GROUP_BYTES], FP8)
        pattern = sb("pattern", [H, C // GC, MATS, PERIOD], FP8)
        signs = sb("signs", [H, SIGN_BUFS, W + 2, GC], FP8)
        stats = sb("stats", [H, SLOTS, GROUPS], F32)
        unread = sb("unread", [H, 2, W, GC], U8)
        averager = sb("averager", [H, H], F32)
        in_band = sb("in_band", [H, H], F32)
        mask = sb("mask", [H, H], U8)

        conv = [ctx.enter_context(nc.psum_tensor(f"conv{i}", [FULL, GC, FULL], F32))
                for i in range(CONV_BUFS)]
        averages = [ctx.enter_context(nc.psum_tensor(f"averages{q}", [H, 512], F32))
                    for q in range(2)]

        loaded = [sem(f"loaded{s}") for s in range(SLOTS)]
        stored = [[sem(f"stored{s}_{j}") for j in range(CHUNKS)] for s in range(SLOTS)]
        taps_cleared = sem("taps_cleared")
        taps_loaded = sem("taps_loaded")
        averager_ready = sem("averager_ready")
        borders_ready = sem("borders_ready")
        mask_step = sem("mask_step")
        pads_ready = sem("pads_ready")
        pattern_step = sem("pattern_step")
        bands_ready = sem("bands_ready")
        sums_ready = sem("sums_ready")
        averages_ready = sem("averages_ready")
        means_ready = sem("means_ready")
        signs_ready = sem("signs_ready")
        conv_ready = sem("conv_ready")
        added = sem("added")

        taps = bands[:, 0:PERIOD * TC * 4].bitcast(F32).rearrange("p (x j) -> p x j", x=PERIOD)
        band_words = bands[:, :].bitcast(U32).rearrange("p (g n) -> p g n", g=GROUPS)
        pattern_words = pattern[:, :, :, :].rearrange("p g m b -> p g (m b)").bitcast(U32)
        mask_words = mask[:, :].bitcast(U32)
        PW = PERIOD // 4

        block = ctx.enter_context(nc.Block())

        def dram_chunk(t, u, j):
            half, image = u // IMAGES, u % IMAGES
            if isinstance(u, int):
                return t[image, :, j * CW:(j + 1) * CW, half * HC:(half + 1) * HC]
            return t[bass.ds(image, 1), :, j * CW:(j + 1) * CW,
                     bass.ds(half * HC, HC)].rearrange("a h w c -> (a h) w c")

        @block.sync
        def _(sp):
            def load(u, slot, j):
                sp.dma_start(slots[:, slot, j * CW:(j + 1) * CW, :],
                             dram_chunk(x, u, j)).then_inc(loaded[slot], 16)

            def store(u, slot, j):
                sp.dma_start(dram_chunk(out, u, j),
                             slots[:, slot, j * CW:(j + 1) * CW, :]).then_inc(stored[slot][j], 16)

            def turn(u, slot, round_, refill):
                sp.wait_ge(added, GROUPS * (u + 1))
                for j in range(CHUNKS + STORE_LEAD):
                    if j < CHUNKS:
                        store(u, slot, j)
                    k = j - STORE_LEAD
                    if refill and k >= 0:
                        sp.wait_ge(stored[slot][k], 16 * (round_ + 1))
                        load(u + SLOTS, slot, k)

            for j in range(FIRST_CHUNKS):
                load(0, 0, j)
            sp.wait_ge(taps_cleared, 2)
            for r in range(PERIOD):
                rows = taps[r:H:PERIOD, :, :]
                for dh_hi, dh_lo in (((0, 0), (1, 2)) if r == PERIOD - 1 else
                                     ((0, 1), (2, 2)) if r == 0 else ((0, 2),)):
                    places = range((r + 1 - dh_lo) % PERIOD, (r + 1 - dh_hi) % PERIOD + 1)
                    src = kern_rows[dh_lo:(dh_hi - 1 if dh_hi else None):-1, :]
                    sp.dma_start(rows[:, places[0]:places[-1] + 1, :],
                                 src.unsqueeze(0).to_broadcast([H // PERIOD, len(places), TC])
                                 ).then_inc(taps_loaded, 16)
            for u in range(SLOTS):
                for j in range(FIRST_CHUNKS if u == 0 else 0, CHUNKS):
                    load(u, u, j)
            refills = UNITS - SLOTS
            rounds = refills // SLOTS
            with sp.Fori(0, rounds) as r:
                for s in range(SLOTS):
                    turn(r * SLOTS + s, s, r, True)
            for u in range(rounds * SLOTS, UNITS):
                turn(u, u % SLOTS, u // SLOTS, u < refills)
            for s in range(SLOTS):
                for j in range(CHUNKS):
                    sp.wait_ge(stored[s][j], 16 * len(range(s, UNITS, SLOTS)))

        @block.gpsimd
        def _(pool):
            nc.gpsimd.memset(taps[:, 0:PERIOD // 2, :], 0.0).then_inc(taps_cleared, 1)
            nc.gpsimd.memset(averager[:, :], 1.0 / (H * W * GC)).then_inc(averager_ready, 1)
            nc.gpsimd.memset(in_band[:, :], 255.0).then_inc(mask_step, 1)
            pool.wait_ge(mask_step, 1)
            nc.gpsimd.affine_select(out=in_band[:, :], in_=in_band[:, :], compare_op=ALU.is_ge,
                                    fill=0.0, base=1, pattern=[[1, H]],
                                    channel_multiplier=-1).then_inc(mask_step, 1)
            pool.wait_ge(mask_step, 2)
            nc.gpsimd.affine_select(out=in_band[:, :], in_=in_band[:, :], compare_op=ALU.is_ge,
                                    fill=0.0, base=1, pattern=[[-1, H]],
                                    channel_multiplier=1).then_inc(mask_step, 1)
            pool.wait_ge(mask_step, 3)
            nc.gpsimd.tensor_copy(mask[:, :], in_band[:, :]).then_inc(mask_step, 1)
            for b in range(SIGN_BUFS):
                nc.gpsimd.memset(signs[:, b, 0, :], 0.0)
                nc.gpsimd.memset(signs[:, b, W + 1, :], 0.0).then_inc(borders_ready, 1)

        @block.scalar
        def _(act):
            def pair_means(u, slot, q):
                act.wait_ge(averages_ready, u * PAIRS + q + 1)
                nc.scalar.copy(stats[:, slot, q * PAIR:(q + 1) * PAIR],
                               averages[q % 2][:, 0:PAIR]).then_inc(means_ready, 1)

            def unit_sums(u, slot, round_, after_first=True):
                act.wait_ge(loaded[slot], 16 * CHUNKS * (round_ + 1))
                for g in range(GROUPS):
                    if after_first or g >= 2:
                        act.wait_ge(sums_ready, u * GROUPS + g - 1)
                    nc.scalar.activation(unread[:, g % 2, :, :],
                                         slots[:, slot, :, g * GC:(g + 1) * GC], ACT.Copy,
                                         accum_out=stats[:, slot, g:g + 1]).then_inc(sums_ready, 1)
                    if g % PAIR == PAIR - 1:
                        pair_means(u, slot, g // PAIR)

            for u in range(SLOTS):
                unit_sums(u, u, 0, after_first=u > 0)
            with act.Fori(1, UNITS // SLOTS) as r:
                for s in range(SLOTS):
                    unit_sums(r * SLOTS + s, s, r)
            for u in range(UNITS // SLOTS * SLOTS, UNITS):
                unit_sums(u, u % SLOTS, u // SLOTS)


        @block.tensor
        def _(pe):
            pe.wait_ge(averager_ready, 1)
            pe.wait_ge(borders_ready, SIGN_BUFS)
            pe.wait_ge(pads_ready, 1)

            def pair_averages(u, slot, q):
                pe.wait_ge(sums_ready, u * GROUPS + PAIR * (q + 1))
                nc.tensor.matmul(averages[q % 2][:, 0:PAIR], averager[:, :],
                                 stats[:, slot, q * PAIR:(q + 1) * PAIR],
                                 start=True, stop=True).then_inc(averages_ready, 1)

            def unit(u, slot, after_first=True, last=False):
                half = u // IMAGES
                for g in range(GROUPS):
                    n = u * GROUPS + g
                    if g % PAIR == PAIR - MEAN_LEAD:
                        if g < GROUPS - MEAN_LEAD:
                            pair_averages(u, slot, g // PAIR + 1)
                        elif not last:
                            pair_averages(u + 1, (slot + 1) % SLOTS, 0)
                    pe.wait_ge(bands_ready, half * GROUPS + g + 1)
                    pe.wait_ge(signs_ready, n + 1)
                    if after_first or g >= CONV_BUFS:
                        pe.wait_ge(added, n + 1 - CONV_BUFS)
                    pe.nop(nofuse=True)
                    sums_to = conv[(slot * GROUPS + g) % CONV_BUFS]
                    for c in range(GC):
                        for dw in range(TAPS):
                            at = g * GROUP_BYTES + (dw * GC + c) * H
                            product = nc.tensor.matmul(sums_to[:, c, 0:W],
                                                       bands[:, at:at + FULL],
                                                       signs[:, g % SIGN_BUFS, dw:dw + W, c],
                                                       start=dw == 0, stop=dw == TAPS - 1)
                    product.then_inc(conv_ready, 1)

            pair_averages(0, 0, 0)
            unit(0, 0, after_first=False)
            lead = (UNITS - 2) // SLOTS * SLOTS
            with pe.Fori(0, lead // SLOTS) as r:
                for s in range(SLOTS):
                    unit(r * SLOTS + s + 1, (s + 1) % SLOTS)
            for u in range(lead + 1, UNITS):
                unit(u, u % SLOTS, last=u == UNITS - 1)

        @block.vector
        def _(dve):
            nc.vector.memset(taps[:, PERIOD // 2:, :], 0.0).then_inc(taps_cleared, 1)
            dve.wait_ge(taps_loaded, 16 * (PERIOD + 2))
            nc.vector.tensor_scalar(taps[:, :, :], taps[:, :, :], 0.0, 4.0,
                                    ALU.is_ge, ALU.mult).then_inc(pattern_step, 1)
            dve.wait_ge(pattern_step, 1)
            for dw in range(TAPS):
                nc.vector.tensor_scalar(
                    pattern[:, :, dw * GC:(dw + 1) * GC, :],
                    taps[:, :, dw * C:(dw + 1) * C].rearrange("p x (g c) -> p g c x", c=GC),
                    2.0, None, ALU.subtract, saturate=False).then_inc(pattern_step, 1)
            dve.wait_ge(pattern_step, 1 + TAPS)
            pads = band_words[:, :, MATS * H // 4:]
            nc.vector.memset(pads, 0).then_inc(pads_ready, 1)
            dve.wait_ge(mask_step, 4)

            def build(half, g):
                dst = band_words[:, g, 0:MATS * H // 4].rearrange("p (m a b) -> p m a b",
                                                                  m=MATS, b=PW)
                src = pattern_words[:, half * GROUPS + g, :].rearrange("p (m b) -> p m b", b=PW)
                src = src.unsqueeze(2).to_broadcast([H, MATS, H // PERIOD, PW])
                msk = mask_words.rearrange("p (a b) -> p a b", b=PW)
                msk = msk.unsqueeze(1).to_broadcast([H, MATS, H // PERIOD, PW])
                nc.vector.tensor_tensor(dst, msk, src, ALU.bitwise_and).then_inc(bands_ready, 1)

            def sign(u, slot, g):
                if g % PAIR == 0:
                    dve.wait_ge(means_ready, u * PAIRS + g // PAIR + 1)
                    dve.nop(nofuse=True)
                nc.vector.tensor_scalar(signs[:, g % SIGN_BUFS, 1:W + 1, :],
                                        slots[:, slot, :, g * GC:(g + 1) * GC],
                                        stats[:, slot, g:g + 1], 0.5,
                                        ALU.is_ge, ALU.subtract,
                                        saturate=False).then_inc(signs_ready, 1)

            def add(u, slot, g):
                dve.wait_ge(conv_ready, u * GROUPS + g + 1)
                here = slots[:, slot, :, g * GC:(g + 1) * GC]
                buffer = conv[(slot * GROUPS + g) % CONV_BUFS]
                nc.vector.tensor_tensor(here, here, buffer[0:H, :, 0:W].rearrange("p c w -> p w c"),
                                        ALU.add).then_inc(added, 1)

            def unit(u, slot, build_next=False, last=False):
                for g in range(GROUPS):
                    ahead = g + LEAD
                    if ahead < GROUPS:
                        sign(u, slot, ahead)
                    elif not last:
                        sign(u + 1, (slot + 1) % SLOTS, ahead - GROUPS)
                    add(u, slot, g)
                    if build_next:
                        build(1, g)

            for g in range(GROUPS):
                build(0, g)
            for g in range(LEAD):
                sign(0, 0, g)
            unit(0, 0)
            first = IMAGES - 1
            loops = (first - 1) // SLOTS
            with dve.Fori(0, loops) as r:
                for s in range(SLOTS):
                    unit(r * SLOTS + (s + 1), (s + 1) % SLOTS)
            for u in range(loops * SLOTS + 1, first + 1):
                unit(u, u % SLOTS, build_next=u == first)
            loops = (UNITS - 1 - IMAGES) // SLOTS
            with dve.Fori(0, loops) as r:
                for s in range(SLOTS):
                    unit(r * SLOTS + (IMAGES + s), (IMAGES + s) % SLOTS)
            for u in range(IMAGES + loops * SLOTS, UNITS):
                unit(u, u % SLOTS, last=u == UNITS - 1)


def kernel(x, L0_conv_kernel):
    import numpy as np
    import concourse.bacc as bacc
    from concourse.bass_utils import run_bass_kernel_spmd

    nc = bacc.Bacc("TRN2", target_bir_lowering=False, num_devices=1, dynamic_dma_scratch_size=1024)
    arrays = {"x_dram": np.ascontiguousarray(x), "kern_dram": np.ascontiguousarray(L0_conv_kernel)}
    ins = [nc.dram_tensor(n, a.shape, mybir.dt.from_np(a.dtype), kind="ExternalInput").ap()
           for n, a in arrays.items()]
    out = nc.dram_tensor("out_dram", x.shape, F32, kind="ExternalOutput").ap()
    conv_preact(nc, *ins, out)
    r = run_bass_kernel_spmd(nc, [arrays], core_ids=[0])
    return r.results[0]["out_dram"]
```
